# Optimizing a Trainium2 kernel written in Bass

```python
import numpy as np
import jax
import jax.numpy as jnp

def _softmax(x, axis=-1):
    return jax.nn.softmax(x, axis=axis)

def _gelu(x):
    return jax.nn.gelu(x, approximate=True)

def _silu(x):
    return jax.nn.silu(x)

def _sigmoid(x):
    return jax.nn.sigmoid(x)

def _layernorm(x, axis=-1, eps=1e-05):
    m = jnp.mean(x, axis=axis, keepdims=True)
    v = jnp.var(x, axis=axis, keepdims=True)
    return (x - m) / jnp.sqrt(v + eps)

def _scatter_add(tgt, idx, src, axis=0):
    return tgt.at[idx].add(src)

def _segment_sum(src, seg, n):
    return jax.ops.segment_sum(src, seg, n)
kernel_name = 'mk_rec_standalone_d1_rec_r8_338394'

def setup_inputs(seed: int=0):
    np.random.seed(seed)
    _w = jnp.asarray

    def _rec_inputs():
        import jax
        import jax.numpy as jnp
        _rk = jax.random.key(seed)
        r_dense_features = -0.000520686 + 1.00062 * jax.random.normal(jax.random.fold_in(_rk, 1), (2048, 512), jnp.float32)
        r_sparse_features = jax.random.randint(jax.random.fold_in(_rk, 2), (26, 2048, 50), 0, 12500, jnp.int32)
        return (r_dense_features, r_sparse_features)
    r_dense_features, r_sparse_features = _rec_inputs()

    def _L0_rec_setup():
        import jax, jax.numpy as jnp
        import numpy as np
        NUM_TABLES = 26
        NUM_EMB = 12500
        EMB_DIM = 64
        DENSE_DIM = 512
        BATCH = 512
        BAG = 50
        HIDDEN_OUT = 512

        def _mlp(x, w1, b1, w2, b2):
            h = jax.nn.relu(x @ w1.T + b1)
            return jax.nn.relu(h @ w2.T + b2)
        key = jax.random.key(seed)
        ks = jax.random.split(key, 12)
        dense_features = jax.random.normal(ks[0], (BATCH, DENSE_DIM), dtype=jnp.float32)
        sparse_features = jax.random.randint(ks[1], (NUM_TABLES, BATCH, BAG), 0, NUM_EMB, dtype=jnp.int64)
        emb_tables = jax.random.normal(ks[2], (NUM_TABLES, NUM_EMB, EMB_DIM), dtype=jnp.float32) * 0.01
        d_w1 = jax.random.normal(ks[3], (DENSE_DIM, DENSE_DIM), dtype=jnp.float32) * (1.0 / np.sqrt(DENSE_DIM))
        d_b1 = jnp.zeros((DENSE_DIM,), dtype=jnp.float32)
        d_w2 = jax.random.normal(ks[4], (EMB_DIM, DENSE_DIM), dtype=jnp.float32) * (1.0 / np.sqrt(DENSE_DIM))
        d_b2 = jnp.zeros((EMB_DIM,), dtype=jnp.float32)
        feat_dim = EMB_DIM * NUM_TABLES + EMB_DIM
        o_w1 = jax.random.normal(ks[5], (HIDDEN_OUT, feat_dim), dtype=jnp.float32) * (1.0 / np.sqrt(feat_dim))
        o_b1 = jnp.zeros((HIDDEN_OUT,), dtype=jnp.float32)
        o_w2 = jax.random.normal(ks[6], (1, HIDDEN_OUT), dtype=jnp.float32) * (1.0 / np.sqrt(HIDDEN_OUT))
        o_b2 = jnp.zeros((1,), dtype=jnp.float32)
        return dict(dense_features=dense_features, sparse_features=sparse_features, emb_tables=emb_tables, d_w1=d_w1, d_b1=d_b1, d_w2=d_w2, d_b2=d_b2, o_w1=o_w1, o_b1=o_b1, o_w2=o_w2, o_b2=o_b2)
    _L0_rec_all = _L0_rec_setup()
    _L0_rec_in = {k: v for k, v in _L0_rec_all.items() if k in ('emb_tables', 'd_w1', 'd_b1', 'd_w2', 'd_b2', 'o_w1', 'o_b1', 'o_w2', 'o_b2')}
    del _L0_rec_all
    return {'r_dense_features': r_dense_features, 'r_sparse_features': r_sparse_features, 'L0_rec_emb_tables': _L0_rec_in['emb_tables'], 'L0_rec_d_w1': _L0_rec_in['d_w1'], 'L0_rec_d_b1': _L0_rec_in['d_b1'], 'L0_rec_d_w2': _L0_rec_in['d_w2'], 'L0_rec_d_b2': _L0_rec_in['d_b2'], 'L0_rec_o_w1': _L0_rec_in['o_w1'], 'L0_rec_o_b1': _L0_rec_in['o_b1'], 'L0_rec_o_w2': _L0_rec_in['o_w2'], 'L0_rec_o_b2': _L0_rec_in['o_b2']}

def reference(r_dense_features, r_sparse_features, L0_rec_emb_tables, L0_rec_d_w1, L0_rec_d_b1, L0_rec_d_w2, L0_rec_d_b2, L0_rec_o_w1, L0_rec_o_b1, L0_rec_o_w2, L0_rec_o_b2):
    import jax
    import jax.numpy as jnp

    def _L0_rec_ref(dense_features, sparse_features, emb_tables, d_w1, d_b1, d_w2, d_b2, o_w1, o_b1, o_w2, o_b2):
        import jax, jax.numpy as jnp
        import numpy as np
        NUM_TABLES = 26
        NUM_EMB = 12500
        EMB_DIM = 64
        DENSE_DIM = 512
        BATCH = 512
        BAG = 50
        HIDDEN_OUT = 512

        def _mlp(x, w1, b1, w2, b2):
            h = jax.nn.relu(x @ w1.T + b1)
            return jax.nn.relu(h @ w2.T + b2)
        dense_x = _mlp(dense_features, d_w1, d_b1, d_w2, d_b2)
        pooled = jax.vmap(lambda tbl, idx: jnp.take(tbl, idx, axis=0).sum(axis=1))(emb_tables, sparse_features)
        B = dense_features.shape[0]
        emb_x = jnp.transpose(pooled, (1, 0, 2)).reshape(B, -1)
        features = jnp.concatenate([dense_x, emb_x], axis=1)
        logits = _mlp(features, o_w1, o_b1, o_w2, o_b2)
        return logits
    y = _L0_rec_ref(r_dense_features, r_sparse_features, L0_rec_emb_tables, L0_rec_d_w1, L0_rec_d_b1, L0_rec_d_w2, L0_rec_d_b2, L0_rec_o_w1, L0_rec_o_b1, L0_rec_o_w2, L0_rec_o_b2)
    return y

_drawn_inputs = setup_inputs


def setup_inputs(seed=0):
    import zlib

    import numpy as np

    out = dict(_drawn_inputs(seed))
    spreads = {'L0_rec_d_b1': (0.0, 0.1), 'L0_rec_d_b2': (0.0, 0.1), 'L0_rec_o_b1': (0.0, 0.1)}
    factors = {}
    for name, (base, spread) in spreads.items():
        noise = np.random.default_rng([zlib.crc32(name.encode()), seed]).standard_normal(out[name].shape)
        drawn = base * np.exp(spread * noise) if base else spread * noise
        out[name] = jnp.asarray(drawn.astype(out[name].dtype))
    for name, factor in factors.items():
        out[name] = (out[name] * factor).astype(out[name].dtype)
    return out
```

```python
from contextlib import ExitStack

import concourse.bass as bass
from concourse import mybir

P = 128
ALU = mybir.AluOpType
ACT = mybir.ActivationFunctionType
AXX = mybir.AxisListType.X
F32 = mybir.dt.float32
BF16 = mybir.dt.bfloat16
U16 = mybir.dt.uint16
I32 = mybir.dt.int32


def build(nc, dense, sparse, tables, d_w1, d_b1, d_w2, d_b2, o_w1, o_b1, o_w2, o_b2, out):
    NT, NV, D = tables.shape
    _, NB, BAG = sparse.shape
    DI = dense.shape[1]
    HID = o_w1.shape[0]
    FEAT = o_w1.shape[1]
    assert NB % (2 * 8 * P) == 0 and NT % 2 == 0 and FEAT == D * (NT + 1) and 2 * D == P
    assert 2 * BAG <= P and HID == 512 and DI == 512

    LOW = -(-NV // P)
    TAIL = NV - (P - 1) * LOW
    UNITS = NB // P
    PAIRS = P // 2
    CHUNKS = 8
    CP = PAIRS // CHUNKS
    BLK = PAIRS // 4
    SLOTS = 3
    PARTS = 3 * D
    QK = NB // 2 // P
    HALF = 64
    BIAS_ROW = HALF + BAG
    K1 = BIAS_ROW + 2
    OFFSET = 0x4B00
    PAD = 1 << 14
    UT = NT * UNITS
    LOOPED = NT - 4
    DVE_CHUNKS = [3]
    ACT_CHUNKS = [c for c in range(CHUNKS) if c not in DVE_CHUNKS]
    NA, ND = len(ACT_CHUNKS), len(DVE_CHUNKS)

    scratch = nc.dram_tensor("pooled_scratch", [NB, NT * D], F32).ap()

    sparse_v = sparse.rearrange("t (k q s) j -> t q k (s j)", q=P, k=QK, s=2)

    with ExitStack() as ctx:
        def sb(name, shape, dt):
            return ctx.enter_context(nc.sbuf_tensor(name, shape, dt))

        def sem(name):
            return ctx.enter_context(nc.semaphore(name))

        parts = sb("parts", [P, 2, LOW, PARTS], BF16)
        rawbuf = sb("rawbuf", [P, 4 * FEAT], F32)
        raw = rawbuf[:, 0:LOW * D].rearrange("p (l d) -> p l d", d=D)
        counts = sb("counts", [P, 2, LOW, P], BF16)
        hot_high = sb("hot_high", [P, 2, BLK, P, 2], BF16)
        hot_low = sb("hot_low", [P, 2, BLK, LOW, 2], BF16)
        idx_raw = sb("idx_raw", [P, QK, 2, BAG], I32)
        idx_pad = sb("idx_pad", [P, QK, 2, HALF], U16)
        idx_t = sb("idx_t", [P, 2, QK * P], U16)
        high = sb("high", [P, 2, QK * P], U16)
        low = sb("low", [P, 2, QK * P], U16)
        iota_i = sb("iota_i", [P, P, 2], I32)
        iota = sb("iota", [P, P, 2], U16)
        ident_b = sb("ident_b", [P, P], BF16)
        ident_f = sb("ident_f", [P, P], F32)
        bias_col = sb("bias_col", [P, 1], F32)
        act_bias = sb("act_bias", [P, 1], F32)
        pooled = sb("pooled", [P, 2, D], F32)
        b1 = sb("b1", [P, 4], F32)
        b2 = sb("b2", [D, 1], F32)
        ob1 = sb("ob1", [P, 4], F32)
        ob2 = sb("ob2", [1, 1], F32)
        ow2 = sb("ow2", [P, 4], F32)
        y = sb("y", [1, 512], F32)

        slots = ctx.enter_context(nc.psum_tensor("slots", [P, SLOTS, 2, 512], F32))
        acc = [ctx.enter_context(nc.psum_tensor(f"acc{i}", [P, 512], F32)) for i in range(2)]
        idx_ps = slots[:, 2, 0, :].bitcast(BF16)

        consts_ready = sem("consts_ready")
        idx_loaded = sem("idx_loaded")
        idx_padded = sem("idx_padded")
        idx_transposed = sem("idx_transposed")
        idx_copied = sem("idx_copied")
        idx_split = sem("idx_split")
        table_loaded = sem("table_loaded")
        table_split = sem("table_split")
        ident_set = sem("ident_set")
        tails_set = sem("tails_set")
        first_split = sem("first_split")
        pool_turn = sem("pool_turn")
        raw_set = sem("raw_set")
        bias_set = sem("bias_set")
        digit_set = sem("digit_set")
        low_hot = sem("low_hot")
        hot_ready = sem("hot_ready")
        chunk_counted = sem("chunk_counted")
        act_evacuated = sem("act_evacuated")
        dve_evacuated = sem("dve_evacuated")
        unit_summed = sem("unit_summed")
        parts_added = sem("parts_added")
        stored = [sem(f"stored{i}") for i in range(2)]
        biases_loaded = sem("biases_loaded")
        w_loaded = sem("w_loaded")
        dw_loaded = sem("dw_loaded")
        nat_loaded = sem("nat_loaded")
        bank_transposed = sem("bank_transposed")
        act_copied = sem("act_copied")
        dve_copied = sem("dve_copied")
        product_ready = sem("product_ready")
        layer_out = sem("layer_out")
        y_stored = sem("y_stored")

        block = ctx.enter_context(nc.Block())

        flat = parts[:, :, :, :].rearrange("p a l c -> p (a l c)").bitcast(F32)
        NBLK = NT // 2 + 1
        o1 = 0
        ow1_t = flat[:, o1:o1 + NBLK * HID].rearrange("p (b o) -> p b o", b=NBLK)
        o1 += NBLK * HID
        dw1_t = flat[:, o1:o1 + 4 * DI].rearrange("p (b o) -> p b o", b=4)
        o1 += 4 * DI
        dw2_t = flat[:, o1:o1 + 4 * D].rearrange("p (b o) -> p b o", b=4)
        o1 += 4 * D
        feat_t = flat[:, o1:o1 + (NBLK - 1) * 512].rearrange("p (b n) -> p b n", n=512)
        o1 += (NBLK - 1) * 512
        assert o1 <= LOW * PARTS
        dense_hid = hot_high[:, :, :, :, :].rearrange("p a b c e -> p (a b c e)").bitcast(F32)
        hid = dense_hid[:, 4 * 512:8 * 512].rearrange("p (b n) -> p b n", n=512)
        dense_hid = dense_hid[:, 0:4 * 512].rearrange("p (b n) -> p b n", n=512)
        spare = hot_low[:, :, :, :, :].rearrange("p a b c e -> p (a b c e)").bitcast(F32)
        dense_out = spare[0:D, 0:512]
        dw2_n = spare[0:D, 512:1024]
        cflat = counts[:, :, :, :].rearrange("p a l c -> p (a l c)").bitcast(F32)
        feat_n = cflat[:, 0:4 * NT * D].rearrange("p (b f) -> p b f", b=4)
        x_n = cflat[:, 4 * NT * D:4 * NT * D + 4 * DI].rearrange("p (b f) -> p b f", b=4)
        x_t = cflat[:, 4 * NT * D + 4 * DI:4 * NT * D + 8 * DI].rearrange("p (b n) -> p b n", b=4)
        assert 4 * NT * D + 8 * DI <= LOW * P
        ow1_n = rawbuf[:, 0:4 * FEAT].rearrange("p (b f) -> p b f", b=4)
        dw1_n = feat_n[:, :, 0:DI]
        SUPERS = NB // 512
        SPLITS = 8
        IDENT, BIASES, CONSTS = 3, 6, 9
        TAIL_ROWS = slice(96, P)
        FIRST = 72
        W_BANKS = NBLK + 4 + 2
        X_BANKS = 4 + NBLK - 1

        def unit(tp, par, g2, k):
            return (2 * tp + par) * UNITS + 2 * g2 + k

        def last_user(c):
            return (0, c - SLOTS) if c >= SLOTS else (1, max(e for e in range(CHUNKS) if e % SLOTS == c))

        def chunk_src(c):
            return slots[:, c % SLOTS, :, :].rearrange("p b n -> p (b n)").bitcast(U16) \
                .rearrange("p (i l s) -> p l i s", i=CP, s=2)[:, 0:LOW, :, :]

        def chunk_dst(k, c):
            return counts[:, k, :, 2 * CP * c:2 * CP * (c + 1)].rearrange("p l (i s) -> p l i s", s=2)

        def mlp_bank(i):
            return slots[:, (i % 4) // 2, i % 2, :]

        def weight_copy(i):
            if i < NBLK:
                rows = D if i == 0 else P
                return mlp_bank(i)[0:rows, :], ow1_t[0:rows, i, :]
            if i < NBLK + 4:
                return mlp_bank(i), dw1_t[:, i - NBLK, :]
            j = 2 * (i - NBLK - 4)
            return mlp_bank(i)[:, 0:2 * D], dw2_t[:, j:j + 2, :].rearrange("p b o -> p (b o)")

        def input_dst(i):
            return x_t[:, i, :] if i < 4 else feat_t[:, i - 4, :]

        @block.sync
        def _(sp):
            def load_idx(t):
                sp.dma_start(idx_raw[:, :, :, :].rearrange("p k s j -> p k (s j)"), sparse_v[t]).then_inc(idx_loaded, 16)

            def load_table(t):
                for a, b in ((0, 112), (112, P - 1)):
                    sp.dma_start(raw[a:b, :, :], tables[t][a * LOW:b * LOW, :].rearrange("(p l) d -> p l d", l=LOW)) \
                      .then_inc(table_loaded, 16)
                sp.dma_start(raw[P - 1:P, 0:TAIL, :], tables[t][(P - 1) * LOW:NV, :].unsqueeze(0)).then_inc(table_loaded, 16)

            def store(t, u, row, k):
                sp.wait_ge(parts_added, u + 1)
                sp.dma_start(scratch[bass.ds(row, P), bass.ds(t * D, D)], pooled[:, k, :]).then_inc(stored[k], 16)

            def table(tp, par, idx=True, load=True):
                t = 2 * tp + par
                if load:
                    sp.wait_ge(table_split, SPLITS * (t + 1))
                    load_table(t + 1)
                if idx:
                    sp.wait_ge(idx_padded, t + 3)
                    load_idx(t + 3)
                with sp.Fori(0, UNITS // 2) as g2:
                    for k in range(2):
                        store(t, unit(tp, par, g2, k), (2 * g2 + k) * P, k)

            load_idx(0)
            sp.wait_ge(raw_set, 1)
            load_table(0)
            for t in (1, 2):
                sp.wait_ge(idx_padded, t)
                load_idx(t)
            sp.dma_start(b1[:, :], d_b1.rearrange("(b p) -> p b", p=P), allow_slow_non_contiguous=True).then_inc(biases_loaded, 16)
            sp.dma_start(b2[:, :], d_b2.rearrange("(p a) -> p a", a=1)).then_inc(biases_loaded, 16)
            sp.dma_start(ob1[:, :], o_b1.rearrange("(b p) -> p b", p=P), allow_slow_non_contiguous=True).then_inc(biases_loaded, 16)
            sp.dma_start(ob2[:, :], o_b2.rearrange("(p a) -> p a", a=1)).then_inc(biases_loaded, 16)
            sp.dma_start(ow2[:, :], o_w2.rearrange("a (b p) -> p (a b)", p=P), allow_slow_non_contiguous=True).then_inc(biases_loaded, 16)
            sp.wait_ge(first_split, 4)
            with sp.Fori(0, LOOPED // 2) as tp:
                table(tp, 0)
                table(tp, 1)
            for t in range(LOOPED, NT):
                if t == NT - 1:
                    sp.wait_ge(table_split, SPLITS * NT)
                    sp.dma_start(ow1_n[:, :, :], o_w1.rearrange("(b p) f -> p b f", p=P)).then_inc(w_loaded, 16)
                table(t // 2, t % 2, idx=t + 3 < NT, load=t + 1 < NT)

            sp.wait_ge(unit_summed, UT)
            sp.dma_start(dw1_n[:, :, :], d_w1.rearrange("(b p) f -> p b f", p=P)).then_inc(dw_loaded, 16)
            sp.dma_start(dw2_n[:, :], d_w2[:, :]).then_inc(dw_loaded, 16)
            sp.wait_ge(stored[0], 16 * UT // 2)
            sp.wait_ge(stored[1], 16 * UT // 2)

            def load_super(s):
                sp.dma_start(x_n[:, :, :], dense[bass.ds(s * 512, 512), :].rearrange("(b p) f -> p b f", p=P)).then_inc(nat_loaded, 16)
                sp.dma_start(feat_n[:, :, :], scratch[bass.ds(s * 512, 512), :].rearrange("(b p) f -> p b f", p=P)).then_inc(nat_loaded, 16)

            with sp.Fori(0, SUPERS) as s:
                sp.wait_ge(bank_transposed, W_BANKS + X_BANKS * s)
                load_super(s)
            sp.wait_ge(y_stored, 16 * SUPERS)

        @block.gpsimd
        def _(pool):
            n_const = 0

            def step(ins):
                nonlocal n_const
                n_const += 1
                ins.then_inc(consts_ready, 1)
                pool.wait_ge(consts_ready, n_const)

            def pad_idx(t):
                pool.wait_ge(idx_loaded, 16 * (t + 1))
                pool.sem_inc(pool_turn, 1)
                pool.tensor_copy(idx_pad[:, :, :, 0:BAG], idx_raw[:, :, :, :]).then_inc(idx_padded, 1)

            step(pool.memset(idx_pad[:, :, :, :], PAD))
            pad_idx(0)
            step(pool.memset(ident_b[:, :], 0.0))
            step(pool.affine_select(out=ident_b[:, :], in_=ident_b[:, :], compare_op=ALU.not_equal, fill=1.0,
                                    base=0, pattern=[[-1, P]], channel_multiplier=1))
            assert n_const == IDENT
            step(pool.memset(bias_col[:, :], 0.0))
            for row, value in ((BIAS_ROW, float(1 << 23)), (BIAS_ROW + 1, float(OFFSET))):
                step(pool.affine_select(out=bias_col[:, :], in_=bias_col[:, :], compare_op=ALU.not_equal, fill=value,
                                        base=-row, pattern=[[0, 1]], channel_multiplier=1))
            assert n_const == BIASES
            step(pool.iota(iota_i[:, :, :], pattern=[[1, P], [0, 2]], base=0, channel_multiplier=0))
            step(pool.tensor_copy(iota[:, :, :], iota_i[:, :, :]))
            step(pool.memset(hot_high[TAIL_ROWS, :, :, :, :], 1.0))
            assert n_const == CONSTS

            def split_table(t, par, t_static, since=0):
                pool.wait_ge(table_loaded, 48 * (t + 1))
                if not (t_static is not None and t_static < 2):
                    pool.wait_ge(unit_summed, UNITS * (t - 1))
                middle = (since + LOW) // 2
                for n, rows in enumerate((slice(since, middle), slice(middle, LOW))):
                    x = raw[:, rows, :]
                    hi, mid, lo = (parts[:, par, rows, i * D:(i + 1) * D] for i in range(3))
                    at = SPLITS * t + 4 * n
                    pool.sem_inc(pool_turn, 1)
                    pool.tensor_copy(hi, x).then_inc(table_split, 1)
                    pool.wait_ge(table_split, at + 1)
                    pool.tensor_tensor(x, x, hi, ALU.subtract).then_inc(table_split, 1)
                    pool.wait_ge(table_split, at + 2)
                    pool.sem_inc(pool_turn, 1)
                    pool.tensor_copy(mid, x).then_inc(table_split, 1)
                    pool.wait_ge(table_split, at + 3)
                    pool.tensor_tensor(lo, x, mid, ALU.subtract).then_inc(table_split, 1)
                    pool.wait_ge(table_split, at + 4)

            for t in (1, 2):
                pool.wait_ge(idx_transposed, t)
                pad_idx(t)
            split_table(0, 0, 0, since=FIRST)
            pool.memset(ident_f[:, :], 0.0).then_inc(ident_set, 1)
            pool.wait_ge(ident_set, 1)
            pool.affine_select(out=ident_f[:, :], in_=ident_f[:, :], compare_op=ALU.not_equal, fill=1.0,
                               base=0, pattern=[[-1, P]], channel_multiplier=1).then_inc(ident_set, 1)
            pool.wait_ge(ident_set, 2)

            def table(tp, par, t_static=None, split=True, idx=True):
                t = 2 * tp + par
                if split:
                    split_table(t + 1, 1 - par, None if t_static is None else t_static + 1)
                if idx:
                    pool.wait_ge(idx_transposed, t + 3)
                    pad_idx(t + 3)

            table(0, 0, 0)
            table(0, 1, 1)
            with pool.Fori(1, LOOPED // 2) as tp:
                table(tp, 0)
                table(tp, 1)
            for t in range(LOOPED, NT):
                table(t // 2, t % 2, t, split=t + 1 < NT, idx=t + 3 < NT)

        @block.tensor
        def _(pe):
            def transpose_idx(t):
                pe.wait_ge(idx_padded, t + 1)
                if not isinstance(t, int) or t > 0:
                    pe.wait_ge(idx_copied, t)
                for k in range(QK):
                    last = pe.transpose(idx_ps[:, k * P:(k + 1) * P],
                                        idx_pad[:, k, :, :].rearrange("p s j -> p (s j)").bitcast(BF16), ident_b[:, :])
                last.then_inc(idx_transposed, 1)

            def count_chunk(v, c, first=False, copied=None):
                hf = c // (CHUNKS // 2)
                if c % (CHUNKS // 2) == 0:
                    pe.wait_ge(hot_ready, 2 * v + hf + 1)
                back, lc = last_user(c)
                if not (first and back):
                    who, n, at = (act_evacuated, NA, ACT_CHUNKS) if lc in ACT_CHUNKS else (dve_evacuated, ND, DVE_CHUNKS)
                    pe.wait_ge(who, n * (v - back) + at.index(lc) + 1)
                if c == 2 and copied is not None:
                    pe.wait_ge(idx_copied, copied)
                for i in range(CP):
                    r = CP * c + i - hf * (PAIRS // 2)
                    last = pe.matmul(slots[:, c % SLOTS, i // 4, (i % 4) * P:(i % 4) * P + LOW],
                                     hot_high[0:K1, hf, r // 2, :, r % 2], hot_low[0:K1, hf, r // 2, :, r % 2],
                                     start=True, stop=True)
                last.then_inc(chunk_counted, 1)

            def sum_steps(v, k, tpar, lo, hi):
                for l in range(lo, hi):
                    last = pe.matmul(acc[k][:, 0:PARTS], counts[:, k, l, :], parts[:, tpar, l, :],
                                     start=(l == 0), stop=(l == LOW - 1))
                if hi == LOW:
                    last.then_inc(unit_summed, 1)

            CUT = [0, 0, 10, 20, 38, 52, 66, 78, LOW]

            def iteration(u, k, tpar, t, copied, more=True):
                for c in range(CHUNKS):
                    if more:
                        count_chunk(u + 1, c, copied=copied)
                    if CUT[c] == 0 and CUT[c + 1] > 0:
                        pe.wait_ge(table_split, SPLITS * (t + 1))
                        pe.wait_ge(act_evacuated, NA * (u + 1))
                        pe.wait_ge(dve_evacuated, ND * (u + 1))
                    sum_steps(u, k, tpar, CUT[c], CUT[c + 1])

            def table(tp, par, idx=True, last=False):
                t = 2 * tp + par
                if idx:
                    pe.wait_ge(act_evacuated, NA * unit(tp, par, 0, 0) + ACT_CHUNKS.index(5) + 1)
                    transpose_idx(t + 2)
                copied = t + 3 if idx else None
                loop = UNITS // 2 - (1 if last else 0)
                with pe.Fori(0, loop) as g2:
                    for k in range(2):
                        iteration(unit(tp, par, g2, k), k, par, t, copied)
                if last:
                    iteration(UT - 2, 0, par, t, copied)
                    iteration(UT - 1, 1, par, t, copied, more=False)

            pe.wait_ge(consts_ready, IDENT)
            transpose_idx(0)
            for c in range(CHUNKS):
                count_chunk(0, c, first=True, copied=1)
            pe.wait_ge(act_evacuated, ACT_CHUNKS.index(5) + 1)
            transpose_idx(1)
            pe.wait_ge(first_split, 4)
            with pe.Fori(0, LOOPED // 2) as tp:
                table(tp, 0)
                table(tp, 1)
            for t in range(LOOPED, NT):
                table(t // 2, t % 2, idx=t + 2 < NT, last=t == NT - 1)

            def tbank(i):
                return slots[:, (i % 4) // 2, i % 2, :]

            def transposed(i, prior_act, prior_dve, blocks, rows):
                need = (i - 4) // 2 + 1 if i >= 4 else 0
                done, prior = (act_copied, prior_act) if i % 2 == 0 else (dve_copied, prior_dve)
                if not (isinstance(prior, int) and prior + need == 0):
                    pe.wait_ge(done, prior + need)
                for j, src in enumerate(blocks):
                    n = src.shape[0]
                    last = pe.transpose(tbank(i)[0:rows, j * n:(j + 1) * n], src, ident_f[0:n, 0:n])
                last.then_inc(bank_transposed, 1)

            pe.wait_ge(ident_set, 2)
            pe.wait_ge(w_loaded, 16)
            pe.wait_ge(parts_added, UT)
            n = 0
            for b in range(NBLK):
                cols = slice(0, D) if b == 0 else slice(D + P * (b - 1), D + P * b)
                transposed(n, 0, 0, [ow1_n[:, o, cols] for o in range(4)], D if b == 0 else P)
                n += 1
            pe.wait_ge(dw_loaded, 32)
            for b in range(4):
                transposed(n, 0, 0, [dw1_n[:, o, b * P:(b + 1) * P] for o in range(4)], P)
                n += 1
            for half in range(2):
                transposed(n, 0, 0, [dw2_n[:, (2 * half + j) * P:(2 * half + j + 1) * P] for j in range(2)], P)
                n += 1
            assert n == W_BANKS and W_BANKS % 2 == 0

            pe.wait_ge(biases_loaded, 80)
            out_bank = [slots[:, 2, 0, :], slots[:, 2, 1, :], acc[0][:, :], acc[1][:, :]]
            OUTS = 10
            with pe.Fori(0, SUPERS) as s:
                pe.wait_ge(nat_loaded, 32 * (s + 1))
                for i in range(X_BANKS):
                    src = [x_n[:, b, i * P:(i + 1) * P] for b in range(4)] if i < 4 else \
                          [feat_n[:, b, (i - 4) * P:(i - 3) * P] for b in range(4)]
                    transposed(i, W_BANKS // 2 + (X_BANKS + 1) // 2 * s, W_BANKS // 2 + X_BANKS // 2 * s, src, P)

                def product(m, terms, rows, after=None):
                    if m >= 4:
                        pe.wait_ge(layer_out, OUTS * s + m - 3)
                    for i, (w, x, wait) in enumerate(terms):
                        if wait is not None:
                            pe.wait_ge(layer_out, OUTS * s + wait)
                        last = pe.matmul(out_bank[m % 4][0:rows, :], w, x, start=(i == 0), stop=(i == len(terms) - 1))
                    last.then_inc(product_ready, 1)

                pe.wait_ge(act_copied, W_BANKS // 2 + (X_BANKS + 1) // 2 * (s + 1))
                pe.wait_ge(dve_copied, W_BANKS // 2 + X_BANKS // 2 * (s + 1))
                for o in range(4):
                    product(o, [(dw1_t[:, b, o * P:(o + 1) * P], x_t[:, b, :], None) for b in range(4)], P)
                product(4, [(dw2_t[:, b, :], dense_hid[:, b, :], b + 1) for b in range(4)], D)
                for o in range(4):
                    product(5 + o, [(ow1_t[:, b, o * P:(o + 1) * P], feat_t[:, b - 1, :], None) for b in range(1, NBLK)]
                            + [(ow1_t[0:D, 0, o * P:(o + 1) * P], dense_out, 5)], P)
                product(9, [(ow2[:, b:b + 1], hid[:, b, :], 6 + b) for b in range(4)], 1)

        @block.scalar
        def _(act):
            def copy_idx(t, tpar, ever=True):
                act.wait_ge(idx_transposed, t + 1)
                if ever:
                    act.wait_ge(idx_split, t - 1)
                act.activation(idx_t[:, tpar, :], idx_ps.bitcast(U16), ACT.Copy).then_inc(idx_copied, 1)

            def evacuate(v, k):
                for c in ACT_CHUNKS:
                    act.wait_ge(chunk_counted, CHUNKS * v + c + 1)
                    act.activation(chunk_dst(k, c), chunk_src(c), ACT.Identity, bias=act_bias[:, 0:1]).then_inc(act_evacuated, 1)

            def table(tp, par, idx=True, last=False):
                t = 2 * tp + par
                if idx:
                    copy_idx(t + 2, par)
                with act.Fori(0, UNITS // 2 - (1 if last else 0)) as g2:
                    evacuate(unit(tp, par, g2, 0) + 1, 1)
                    evacuate(unit(tp, par, g2, 1) + 1, 0)
                if last:
                    evacuate(UT - 1, 1)

            act.wait_ge(consts_ready, BIASES)
            act.activation(hot_low[TAIL_ROWS, :, :, :, :].rearrange("p a b l e -> p (a b l e)"),
                           bias_col[TAIL_ROWS, 0:1].to_broadcast([P - 96, 2 * BLK * LOW * 2]), ACT.Copy).then_inc(tails_set, 1)
            act.wait_ge(bias_set, 1)
            copy_idx(0, 0, ever=False)
            evacuate(0, 0)
            copy_idx(1, 1, ever=False)
            with act.Fori(0, LOOPED // 2) as tp:
                table(tp, 0)
                table(tp, 1)
            for t in range(LOOPED, NT):
                table(t // 2, t % 2, idx=t + 2 < NT, last=t == NT - 1)

            act.wait_ge(biases_loaded, 80)
            for i in range(0, W_BANKS, 2):
                act.wait_ge(bank_transposed, i + 1)
                src, dst = weight_copy(i)
                act.activation(dst, src, ACT.Copy).then_inc(act_copied, 1)
            with act.Fori(0, SUPERS) as s:
                for i in range(0, X_BANKS, 2):
                    act.wait_ge(bank_transposed, W_BANKS + X_BANKS * s + i + 1)
                    act.activation(input_dst(i), mlp_bank(i), ACT.Copy).then_inc(act_copied, 1)

                def layer(m, dst, bias, rows):
                    act.wait_ge(product_ready, 10 * s + m + 1)
                    banks = [slots[:, 2, 0, :], slots[:, 2, 1, :], acc[0][:, :], acc[1][:, :]]
                    act.activation(dst, banks[m % 4][0:rows, :], ACT.Relu, bias=bias).then_inc(layer_out, 1)

                for o in range(4):
                    layer(o, dense_hid[:, o, :], b1[:, o:o + 1], P)
                layer(4, dense_out, b2[:, 0:1], D)
                for o in range(4):
                    layer(5 + o, hid[:, o, :], ob1[:, o:o + 1], P)
                layer(9, y[:, :], ob2[:, 0:1], 1)
                act.wait_ge(layer_out, 10 * (s + 1))
                act.dma_start(out[bass.ds(s * 512, 512), :].rearrange("n a -> a n"), y[:, :]).then_inc(y_stored, 16)
                act.wait_ge(y_stored, 16 * (s + 1))

        @block.vector
        def _(dve):
            nset = [0]

            def split_idx(t, tpar):
                dve.wait_ge(idx_copied, t + 1)
                dve.tensor_scalar(high[:, tpar, :], idx_t[:, tpar, :], 1.0 / LOW, -(LOW - 1) / (2 * LOW),
                                  ALU.mult, ALU.add).then_inc(digit_set, 1)
                dve.wait_ge(digit_set, 2 * t + 1)
                dve.scalar_tensor_tensor(low[:, tpar, :], high[:, tpar, :], -float(LOW), idx_t[:, tpar, :],
                                         ALU.mult, ALU.add).then_inc(digit_set, 1)
                dve.wait_ge(digit_set, 2 * (t + 1))
                dve.sem_inc(idx_split, 1)

            def one_hots(n, v, hf, tpar, first, ever=True):
                if ever:
                    dve.wait_ge(chunk_counted, (CHUNKS // 2) * (n - 1))
                rows = slice(0, BIAS_ROW)

                def operands(size, part, dst):
                    a = iota[rows, 0:size, :].unsqueeze(1).to_broadcast([BIAS_ROW, BLK, size, 2])
                    b = part[rows, tpar, bass.ds(first, PAIRS // 2)].rearrange("p (b e) -> p b e", e=2) \
                        .unsqueeze(2).to_broadcast([BIAS_ROW, BLK, size, 2])
                    return dst[rows, hf, :, :, :], a, b

                dve.tensor_tensor(*operands(LOW, low, hot_low), ALU.is_equal).then_inc(low_hot, 1)
                dve.tensor_tensor(*operands(P, high, hot_high), ALU.is_equal)
                b_rows = hot_low[HALF:BIAS_ROW, hf, :, :, :].rearrange("p b l e -> p (b l e)")
                dve.wait_ge(low_hot, n + 1)
                dve.tensor_scalar(b_rows, b_rows, 65536.0, None, ALU.mult).then_inc(hot_ready, 1)

            def evacuate(v, k, c):
                if c not in DVE_CHUNKS:
                    return
                dve.wait_ge(chunk_counted, CHUNKS * v + c + 1)
                dve.tensor_scalar(chunk_dst(k, c), chunk_src(c), float(OFFSET), None, ALU.subtract).then_inc(dve_evacuated, 1)

            def add_parts(u, k, ever=True):
                dve.wait_ge(unit_summed, u + 1)
                if ever:
                    dve.wait_ge(stored[k], 8 * (u - k))
                dve.tensor_reduce(pooled[:, k, :], acc[k][:, 0:PARTS].rearrange("p (s d) -> p d s", s=3), AXX, ALU.add) \
                    .then_inc(parts_added, 1)

            def iteration(u, k, ones, add=True, ever=True):
                one_hots(2 * u + 3, u + 1, 1, *ones[0])
                if add:
                    add_parts(u - 1, 1 - k, ever)
                evacuate(u + 1, 1 - k, 3)
                if ones[1] is not None:
                    one_hots(2 * u + 4, u + 2, 0, *ones[1])

            def first_pair(g2, half, hf):
                return g2 * P + half * PAIRS + hf * (PAIRS // 2)

            def two_units(tp, par, g2, nxt, nth=None):
                iteration(unit(tp, par, g2, 0), 0, [(par, first_pair(g2, 1, 1)), (nxt[0], first_pair(nxt[1], 0, 0))],
                          add=nth != 0, ever=nth is None)
                iteration(unit(tp, par, g2, 1), 1, [(nxt[0], first_pair(nxt[1], 0, 1)), (nxt[0], first_pair(nxt[1], 1, 0))],
                          ever=nth != 0)

            def table(tp, par, split=True, first=False, last=False):
                t = 2 * tp + par
                if split:
                    split_idx(t + 1, 1 - par)
                if first:
                    two_units(0, 0, 0, (0, 1), nth=0)
                    two_units(0, 0, 1, (0, 2), nth=1)
                with dve.Fori(2 if first else 0, UNITS // 2 - 1) as g2:
                    two_units(tp, par, g2, (par, g2 + 1))
                g2 = UNITS // 2 - 1
                if not last:
                    two_units(tp, par, g2, (1 - par, 0))
                else:
                    iteration(UT - 2, 0, [(par, first_pair(g2, 1, 1)), None])
                    add_parts(UT - 2, 0)
                    add_parts(UT - 1, 1)

            dve.memset(act_bias[:, :], -float(OFFSET)).then_inc(bias_set, 1)
            dve.memset(raw[TAIL_ROWS, TAIL:LOW, :], 0.0).then_inc(raw_set, 1)
            split_idx(0, 0)
            dve.wait_ge(consts_ready, CONSTS)
            dve.wait_ge(tails_set, 1)
            one_hots(0, 0, 0, 0, first_pair(0, 0, 0), ever=False)
            one_hots(1, 0, 1, 0, first_pair(0, 0, 1), ever=False)
            dve.wait_ge(table_loaded, 48)
            x = raw[:, 0:FIRST, :]
            hi, mid, lo = (parts[:, 0, 0:FIRST, i * D:(i + 1) * D] for i in range(3))
            dve.tensor_copy(hi, x).then_inc(first_split, 1)
            evacuate(0, 0, 3)
            dve.wait_ge(first_split, 1)
            dve.tensor_tensor(x, x, hi, ALU.subtract).then_inc(first_split, 1)
            dve.wait_ge(first_split, 2)
            dve.tensor_copy(mid, x).then_inc(first_split, 1)
            dve.wait_ge(first_split, 3)
            dve.tensor_tensor(lo, x, mid, ALU.subtract).then_inc(first_split, 1)
            one_hots(2, 1, 0, 0, first_pair(0, 1, 0))
            table(0, 0, first=True)
            table(0, 1)
            with dve.Fori(1, LOOPED // 2) as tp:
                table(tp, 0)
                table(tp, 1)
            for t in range(LOOPED, NT):
                table(t // 2, t % 2, split=t + 1 < NT, last=t == NT - 1)

            for i in range(1, W_BANKS, 2):
                dve.wait_ge(bank_transposed, i + 1)
                src, dst = weight_copy(i)
                dve.tensor_copy(dst, src).then_inc(dve_copied, 1)
            with dve.Fori(0, SUPERS) as s:
                for i in range(1, X_BANKS, 2):
                    dve.wait_ge(bank_transposed, W_BANKS + X_BANKS * s + i + 1)
                    dve.tensor_copy(input_dst(i), mlp_bank(i)).then_inc(dve_copied, 1)


_INS = ['r_dense_features', 'r_sparse_features', 'L0_rec_emb_tables', 'L0_rec_d_w1', 'L0_rec_d_b1', 'L0_rec_d_w2',
        'L0_rec_d_b2', 'L0_rec_o_w1', 'L0_rec_o_b1', 'L0_rec_o_w2', 'L0_rec_o_b2']


def kernel(**inputs):
    import numpy as _np
    import concourse.bacc as _bacc
    from concourse import mybir as _mybir
    from concourse.bass_utils import run_bass_kernel_spmd as _run

    nc = _bacc.Bacc("TRN2", target_bir_lowering=False, num_devices=1)
    arrays, args = {}, []
    for name in _INS:
        a = _np.ascontiguousarray(inputs[name])
        arrays[f"in_{name}_dram"] = a
        args.append(nc.dram_tensor(f"in_{name}_dram", a.shape, _mybir.dt.from_np(a.dtype), kind="ExternalInput").ap())
    rows = inputs['r_dense_features'].shape[0]
    out = nc.dram_tensor("out_0_dram", (rows, 1), _mybir.dt.float32, kind="ExternalOutput").ap()
    build(nc, *args, out)
    r = _run(nc, [arrays], core_ids=[0])
    return r.results[0]["out_0_dram"]
```

```python
from contextlib import ExitStack

import concourse.bass as bass
from concourse import mybir

P = 128
ALU = mybir.AluOpType
ACT = mybir.ActivationFunctionType
AXX = mybir.AxisListType.X
F32 = mybir.dt.float32
BF16 = mybir.dt.bfloat16
U16 = mybir.dt.uint16
I32 = mybir.dt.int32


def build(nc, dense, sparse, tables, d_w1, d_b1, d_w2, d_b2, o_w1, o_b1, o_w2, o_b2, out):
    NT, NV, D = tables.shape
    _, NB, BAG = sparse.shape
    DI = dense.shape[1]
    HID = o_w1.shape[0]
    FEAT = o_w1.shape[1]
    GATHERED = 2
    NS = NT - GATHERED
    assert NB % (2 * 8 * P) == 0 and NS % 2 == 0 and FEAT == D * (NT + 1) and 2 * D == P
    assert 2 * BAG <= P and HID == 512 and DI == 512

    LOW = -(-NV // P)
    TAIL = NV - (P - 1) * LOW
    UNITS = NB // P
    PAIRS = P // 2
    CHUNKS = 8
    CP = PAIRS // CHUNKS
    BLK = PAIRS // 4
    SLOTS = 3
    PARTS = 3 * D
    QK = NB // 2 // P
    HALF = 64
    BIAS_ROW = HALF + BAG
    K1 = BIAS_ROW + 2
    OFFSET = 0x4B00
    PAD = 1 << 14
    UT = NS * UNITS
    GU = GATHERED * UNITS
    ACCS = 8
    GROUP = ACCS // 2
    LOOPED = NS - 4
    DVE_CHUNKS = [3]
    ACT_CHUNKS = [c for c in range(CHUNKS) if c not in DVE_CHUNKS]
    NA, ND = len(ACT_CHUNKS), len(DVE_CHUNKS)

    scratch = nc.dram_tensor("pooled_scratch", [NB, NS * D], F32).ap()
    gathered_scratch = nc.dram_tensor("gathered_scratch", [GATHERED * NB, D], F32).ap()

    sparse_v = sparse.rearrange("t (k q s) j -> t q k (s j)", q=P, k=QK, s=2)

    with ExitStack() as ctx:
        def sb(name, shape, dt):
            return ctx.enter_context(nc.sbuf_tensor(name, shape, dt))

        def sem(name):
            return ctx.enter_context(nc.semaphore(name))

        parts = sb("parts", [P, 2, LOW, PARTS], BF16)
        rawbuf = sb("rawbuf", [P, 4 * FEAT], F32)
        raw = rawbuf[:, 0:LOW * D].rearrange("p (l d) -> p l d", d=D)
        counts = sb("counts", [P, 2, LOW, P], BF16)
        hot_high = sb("hot_high", [P, 2, BLK, P, 2], BF16)
        hot_low = sb("hot_low", [P, 2, BLK, LOW, 2], BF16)
        idx_raw = sb("idx_raw", [P, QK, 2, BAG], I32)
        idx_pad = sb("idx_pad", [P, QK, 2, HALF], U16)
        idx_t = sb("idx_t", [P, 2, QK * P], U16)
        high = sb("high", [P, 2, QK * P], U16)
        low = sb("low", [P, 2, QK * P], U16)
        iota_i = sb("iota_i", [P, P, 2], I32)
        iota = sb("iota", [P, P, 2], U16)
        ident_b = sb("ident_b", [P, P], BF16)
        ident_f = sb("ident_f", [P, P], F32)
        bias_col = sb("bias_col", [P, 1], F32)
        act_bias = sb("act_bias", [P, 1], F32)
        pooled = sb("pooled", [P, 2, D], F32)
        row_accs = rawbuf[:, LOW * D:LOW * D + ACCS * D]
        bag_idx = sb("bag_idx", [P, BAG], I32)
        row_idx = sb("row_idx", [P, BAG], I32)
        table_row = sb("table_row", [P, GU], I32)
        bag_sum = sb("bag_sum", [P, D], F32)
        b1 = sb("b1", [P, 4], F32)
        b2 = sb("b2", [D, 1], F32)
        ob1 = sb("ob1", [P, 4], F32)
        ob2 = sb("ob2", [1, 1], F32)
        ow2 = sb("ow2", [P, 4], F32)
        ones = sb("ones", [P, 1], F32)
        y = sb("y", [1, 512], F32)

        slots = ctx.enter_context(nc.psum_tensor("slots", [P, SLOTS, 2, 512], F32))
        acc = [ctx.enter_context(nc.psum_tensor(f"acc{i}", [P, 512], F32)) for i in range(2)]
        idx_ps = slots[:, 2, 0, :].bitcast(BF16)

        consts_ready = sem("consts_ready")
        idx_loaded = sem("idx_loaded")
        idx_padded = sem("idx_padded")
        idx_transposed = sem("idx_transposed")
        idx_copied = sem("idx_copied")
        idx_split = sem("idx_split")
        table_loaded = sem("table_loaded")
        table_split = sem("table_split")
        ident_set = sem("ident_set")
        tails_set = sem("tails_set")
        first_split = sem("first_split")
        pool_turn = sem("pool_turn")
        raw_set = sem("raw_set")
        bias_set = sem("bias_set")
        digit_set = sem("digit_set")
        low_hot = sem("low_hot")
        bag_idx_loaded = sem("bag_idx_loaded")
        row_idx_ready = sem("row_idx_ready")
        rows_added = [sem(f"rows_added{i}") for i in range(2)]
        accs_added = sem("accs_added")
        bag_sum_stored = sem("bag_sum_stored")
        hot_ready = sem("hot_ready")
        chunk_counted = sem("chunk_counted")
        act_evacuated = sem("act_evacuated")
        dve_evacuated = sem("dve_evacuated")
        unit_summed = sem("unit_summed")
        parts_added = sem("parts_added")
        stored = [sem(f"stored{i}") for i in range(2)]
        biases_loaded = sem("biases_loaded")
        w_loaded = sem("w_loaded")
        dw_loaded = sem("dw_loaded")
        x_loaded = sem("x_loaded")
        feat_loaded = sem("feat_loaded")
        bank_transposed = sem("bank_transposed")
        act_copied = sem("act_copied")
        dve_copied = sem("dve_copied")
        product_ready = sem("product_ready")
        layer_out = sem("layer_out")
        weighted = sem("weighted")
        y_stored = sem("y_stored")

        block = ctx.enter_context(nc.Block())

        flat = parts[:, :, :, :].rearrange("p a l c -> p (a l c)").bitcast(F32)
        NBLK = NT // 2 + 1
        o1 = 0
        ow1_t = flat[:, o1:o1 + NBLK * HID].rearrange("p (b o) -> p b o", b=NBLK)
        o1 += NBLK * HID
        dw1_t = flat[:, o1:o1 + 4 * DI].rearrange("p (b o) -> p b o", b=4)
        o1 += 4 * DI
        dw2_t = flat[:, o1:o1 + 4 * D].rearrange("p (b o) -> p b o", b=4)
        o1 += 4 * D
        feat_t = flat[:, o1:o1 + (NBLK - 1) * 512].rearrange("p (b n) -> p b n", n=512)
        o1 += (NBLK - 1) * 512
        assert o1 <= LOW * PARTS
        dense_hid = hot_high[:, :, :, :, :].rearrange("p a b c e -> p (a b c e)").bitcast(F32)
        hid = dense_hid[:, 4 * 512:8 * 512].rearrange("p (b n) -> p b n", n=512)
        dense_hid = dense_hid[:, 0:4 * 512].rearrange("p (b n) -> p b n", n=512)
        spare = hot_low[:, :, :, :, :].rearrange("p a b c e -> p (a b c e)").bitcast(F32)
        dense_out = spare[0:D, 0:512]
        dw2_n = spare[0:D, 512:1024]
        weighted_sum = spare[:, 1024:1536]
        cflat = counts[:, :, :, :].rearrange("p a l c -> p (a l c)").bitcast(F32)
        x_n = cflat[:, 0:4 * DI].rearrange("p (b f) -> p b f", b=4)
        x_t = cflat[:, 4 * DI:8 * DI].rearrange("p (b n) -> p b n", b=4)
        feat_n = cflat[:, 8 * DI:8 * DI + 4 * NT * D].rearrange("p (b f) -> p b f", b=4)
        assert 4 * NT * D + 8 * DI <= LOW * P and 8 * DI <= LOW * P // 2
        ow1_n = rawbuf[:, 0:4 * FEAT].rearrange("p (b f) -> p b f", b=4)
        dw1_n = hid
        SUPERS = NB // 512
        PIECES = 4
        SPLITS = 4 * PIECES
        IDENT, BIASES, CONSTS = 3, 6, 9
        TAIL_ROWS = slice(96, P)
        FIRST = 64
        W_BANKS = NBLK + 4 + 2
        DENSE_BANKS = 4
        X_BANKS = DENSE_BANKS + NBLK - 1
        X_ACT, X_DVE = (X_BANKS + 1) // 2, X_BANKS // 2
        OUTS = 10

        def unit(tp, par, g2, k):
            return (2 * tp + par) * UNITS + 2 * g2 + k

        def last_user(c):
            return (0, c - SLOTS) if c >= SLOTS else (1, max(e for e in range(CHUNKS) if e % SLOTS == c))

        def chunk_src(c):
            return slots[:, c % SLOTS, :, :].rearrange("p b n -> p (b n)").bitcast(U16) \
                .rearrange("p (i l s) -> p l i s", i=CP, s=2)[:, 0:LOW, :, :]

        def chunk_dst(k, c):
            return counts[:, k, :, 2 * CP * c:2 * CP * (c + 1)].rearrange("p l (i s) -> p l i s", s=2)

        def mlp_bank(i):
            return slots[:, (i % 4) // 2, i % 2, :]

        def weight_copy(i):
            if i < NBLK:
                rows = D if i == 0 else P
                return mlp_bank(i)[0:rows, :], ow1_t[0:rows, i, :]
            if i < NBLK + 4:
                return mlp_bank(i), dw1_t[:, i - NBLK, :]
            j = 2 * (i - NBLK - 4)
            return mlp_bank(i)[:, 0:2 * D], dw2_t[:, j:j + 2, :].rearrange("p b o -> p (b o)")

        def input_dst(i):
            return x_t[:, i, :] if i < DENSE_BANKS else feat_t[:, i - DENSE_BANKS, :]

        def out_bank(m):
            return (slots[:, 2, 0, :], slots[:, 2, 1, :], acc[0][:, :], acc[1][:, :])[m % 4 if m < OUTS - 1 else 3]

        def load_dense(eng, s):
            eng.dma_start(x_n[:, :, :], dense[bass.ds(s * 512, 512), :].rearrange("(b p) f -> p b f", p=P)).then_inc(x_loaded, 16)

        @block.sync
        def _(sp):
            def load_idx(t):
                sp.dma_start(idx_raw[:, :, :, :].rearrange("p k s j -> p k (s j)"), sparse_v[t]).then_inc(idx_loaded, 16)

            def load_table(t):
                for a, b in ((0, 112), (112, P - 1)):
                    sp.dma_start(raw[a:b, :, :], tables[t][a * LOW:b * LOW, :].rearrange("(p l) d -> p l d", l=LOW)) \
                      .then_inc(table_loaded, 16)
                sp.dma_start(raw[P - 1:P, 0:TAIL, :], tables[t][(P - 1) * LOW:NV, :].unsqueeze(0)).then_inc(table_loaded, 16)

            def store(t, u, row, k):
                sp.wait_ge(parts_added, u + 1)
                sp.dma_start(scratch[bass.ds(row, P), bass.ds(t * D, D)], pooled[:, k, :]).then_inc(stored[k], 16)

            def table(tp, par, idx=True, load=True):
                t = 2 * tp + par
                if load:
                    sp.wait_ge(table_split, SPLITS * (t + 1))
                    load_table(t + 1)
                if idx:
                    sp.wait_ge(idx_padded, t + 3)
                    load_idx(t + 3)
                with sp.Fori(0, UNITS // 2) as g2:
                    for k in range(2):
                        store(t, unit(tp, par, g2, k), (2 * g2 + k) * P, k)

            load_idx(0)
            sp.wait_ge(raw_set, 1)
            load_table(0)
            for t in (1, 2):
                sp.wait_ge(idx_padded, t)
                load_idx(t)
            sp.dma_start(b1[:, :], d_b1.rearrange("(b p) -> p b", p=P), allow_slow_non_contiguous=True).then_inc(biases_loaded, 16)
            sp.dma_start(b2[:, :], d_b2.rearrange("(p a) -> p a", a=1)).then_inc(biases_loaded, 16)
            sp.dma_start(ob1[:, :], o_b1.rearrange("(b p) -> p b", p=P), allow_slow_non_contiguous=True).then_inc(biases_loaded, 16)
            sp.dma_start(ob2[:, :], o_b2.rearrange("(p a) -> p a", a=1)).then_inc(biases_loaded, 16)
            sp.dma_start(ow2[:, :], o_w2.rearrange("a (b p) -> p (a b)", p=P), allow_slow_non_contiguous=True).then_inc(biases_loaded, 16)
            sp.wait_ge(first_split, 4)
            with sp.Fori(0, LOOPED // 2) as tp:
                table(tp, 0)
                table(tp, 1)
            for t in range(LOOPED, NS):
                if t == NS - 1:
                    sp.wait_ge(table_split, SPLITS * NS)
                    sp.wait_ge(accs_added, 3 * GU)
                    sp.dma_start(ow1_n[:, :, :], o_w1.rearrange("(b p) f -> p b f", p=P)).then_inc(w_loaded, 16)
                table(t // 2, t % 2, idx=t + 3 < NS, load=t + 1 < NS)

            def load_feat(s):
                sp.dma_start(feat_n[:, :, 0:NS * D], scratch[bass.ds(s * 512, 512), :].rearrange("(b p) f -> p b f", p=P)) \
                  .then_inc(feat_loaded, 16)
                for t in range(GATHERED):
                    sp.dma_start(feat_n[:, :, (NS + t) * D:(NS + t + 1) * D],
                                 gathered_scratch[bass.ds(t * NB + s * 512, 512), :].rearrange("(b p) f -> p b f", p=P)) \
                      .then_inc(feat_loaded, 16)

            sp.wait_ge(unit_summed, UT)
            for k in range(2):
                sp.wait_ge(stored[k], 16 * (UT - UNITS + 512 // P) // 2)
            sp.wait_ge(bag_sum_stored, 16 * GU)
            load_feat(0)
            for k in range(2):
                sp.wait_ge(stored[k], 16 * UT // 2)
            with sp.Fori(0, SUPERS - 1) as s:
                sp.wait_ge(bank_transposed, W_BANKS + X_BANKS * s + DENSE_BANKS)
                load_dense(sp, s + 1)
                sp.wait_ge(bank_transposed, W_BANKS + X_BANKS * s + X_BANKS)
                load_feat(s + 1)
            sp.wait_ge(y_stored, 16 * SUPERS)

        @block.gpsimd
        def _(pool):
            n_const = 0

            def step(ins):
                nonlocal n_const
                n_const += 1
                ins.then_inc(consts_ready, 1)
                pool.wait_ge(consts_ready, n_const)

            def pad_idx(t):
                pool.wait_ge(idx_loaded, 16 * (t + 1))
                pool.sem_inc(pool_turn, 1)
                pool.tensor_copy(idx_pad[:, :, :, 0:BAG], idx_raw[:, :, :, :]).then_inc(idx_padded, 1)

            step(pool.memset(idx_pad[:, :, :, :], PAD))
            pad_idx(0)
            step(pool.memset(ident_b[:, :], 0.0))
            step(pool.affine_select(out=ident_b[:, :], in_=ident_b[:, :], compare_op=ALU.not_equal, fill=1.0,
                                    base=0, pattern=[[-1, P]], channel_multiplier=1))
            assert n_const == IDENT
            step(pool.memset(bias_col[:, :], 0.0))
            for row, value in ((BIAS_ROW, float(1 << 23)), (BIAS_ROW + 1, float(OFFSET))):
                step(pool.affine_select(out=bias_col[:, :], in_=bias_col[:, :], compare_op=ALU.not_equal, fill=value,
                                        base=-row, pattern=[[0, 1]], channel_multiplier=1))
            assert n_const == BIASES
            step(pool.iota(iota_i[:, :, :], pattern=[[1, P], [0, 2]], base=0, channel_multiplier=0))
            step(pool.tensor_copy(iota[:, :, :], iota_i[:, :, :]))
            step(pool.memset(ones[:, :], 1.0))
            assert n_const == CONSTS

            def split_table(t, par, t_static, since=0):
                pool.wait_ge(table_loaded, 48 * (t + 1))
                if not (t_static is not None and t_static < 2):
                    pool.wait_ge(unit_summed, UNITS * (t - 1))
                cuts = [since + (LOW - since) * n // PIECES for n in range(PIECES + 1)]
                for n, rows in enumerate(slice(*cut) for cut in zip(cuts, cuts[1:])):
                    x = raw[:, rows, :]
                    one = ones[:, 0:1].unsqueeze(2).to_broadcast([P, rows.stop - rows.start, D])
                    hi, mid, lo = (parts[:, par, rows, i * D:(i + 1) * D] for i in range(3))
                    at = SPLITS * t + 4 * n
                    pool.tensor_tensor(hi, x, one, ALU.mult).then_inc(table_split, 1)
                    pool.wait_ge(table_split, at + 1)
                    pool.tensor_tensor(x, x, hi, ALU.subtract).then_inc(table_split, 1)
                    pool.wait_ge(table_split, at + 2)
                    pool.tensor_tensor(mid, x, one, ALU.mult).then_inc(table_split, 1)
                    pool.wait_ge(table_split, at + 3)
                    pool.tensor_tensor(lo, x, mid, ALU.subtract).then_inc(table_split, 1)
                    pool.wait_ge(table_split, at + 4)

            pool.wait_ge(idx_transposed, 1)
            pad_idx(1)
            split_table(0, 0, 0, since=FIRST)
            pool.wait_ge(idx_transposed, 2)
            pad_idx(2)
            pool.memset(ident_f[:, :], 0.0).then_inc(ident_set, 1)
            pool.wait_ge(ident_set, 1)
            pool.affine_select(out=ident_f[:, :], in_=ident_f[:, :], compare_op=ALU.not_equal, fill=1.0,
                               base=0, pattern=[[-1, P]], channel_multiplier=1).then_inc(ident_set, 1)
            pool.wait_ge(ident_set, 2)
            pool.iota(table_row[:, :].rearrange("p (t u) -> p t u", t=GATHERED), pattern=[[NV, GATHERED], [0, UNITS]],
                      base=NS * NV, channel_multiplier=0).then_inc(ident_set, 1)
            pool.wait_ge(ident_set, 3)

            all_rows = tables.rearrange("t v d -> (t v) d")
            all_bags = sparse.rearrange("t n j -> (t n) j")
            groups = [range(j, min(j + GROUP, BAG)) for j in range(0, BAG, GROUP)]
            in_half = [sum(len(rows) for rows in groups[h::2]) for h in range(2)]

            pool.dma_start(bag_idx[:, :], all_bags[NS * NB:NS * NB + P, :]).then_inc(bag_idx_loaded, 16)

            def gather(g, more=True):
                pool.wait_ge(bag_idx_loaded, 16 * (g + 1))
                pool.tensor_tensor(row_idx[:, :], bag_idx[:, :], table_row[:, bass.ds(g, 1)].to_broadcast([P, BAG]), ALU.add) \
                    .then_inc(row_idx_ready, 1)
                pool.wait_ge(row_idx_ready, g + 1)
                pool.sem_inc(pool_turn, 1)
                if more:
                    pool.dma_start(bag_idx[:, :], all_bags[bass.ds(NS * NB + (g + 1) * P, P), :]).then_inc(bag_idx_loaded, 16)
                for q, rows in enumerate(groups):
                    if q >= 2:
                        pool.wait_ge(rows_added[q % 2], 16 * (in_half[q % 2] * g + GROUP * (q // 2)))
                        pool.sem_inc(pool_turn, 1)
                    for j in rows:
                        a = j % ACCS
                        pool.indirect_dma_start(row_accs[:, a * D:(a + 1) * D], None, all_rows,
                                                bass.IndirectOffsetOnAxis(ap=row_idx[:, j:j + 1], axis=0),
                                                **({"compute_op": ALU.add} if q >= 2 else {})).then_inc(rows_added[q % 2], 16)
                for h in range(2):
                    pool.wait_ge(rows_added[h], 16 * in_half[h] * (g + 1))
                for n, width in enumerate((ACCS // 2 * D, ACCS // 4 * D, D)):
                    if n == 2 and not (isinstance(g, int) and g == 0):
                        pool.wait_ge(bag_sum_stored, 16 * g)
                    dst = row_accs[:, 0:width] if n < 2 else bag_sum[:, :]
                    pool.tensor_tensor(dst, row_accs[:, 0:width], row_accs[:, width:2 * width], ALU.add).then_inc(accs_added, 1)
                    pool.wait_ge(accs_added, 3 * g + n + 1)
                pool.sem_inc(pool_turn, 1)
                pool.dma_start(gathered_scratch[bass.ds(g * P, P), :], bag_sum[:, :]).then_inc(bag_sum_stored, 16)

            def table(tp, par, t_static=None, split=True, idx=True):
                t = 2 * tp + par
                if split:
                    split_table(t + 1, 1 - par, None if t_static is None else t_static + 1)
                if idx:
                    pool.wait_ge(idx_transposed, t + 3)
                    pad_idx(t + 3)

            looped_units = 3 * (LOOPED // 2 - 1)
            assert 1 + looped_units + NS - LOOPED == GU
            table(0, 0, 0)
            gather(0)
            table(0, 1, 1)
            with pool.Fori(1, LOOPED // 2) as tp:
                table(tp, 0)
                gather(3 * tp - 2)
                gather(3 * tp - 1)
                table(tp, 1)
                gather(3 * tp)
            for t in range(LOOPED, NS):
                table(t // 2, t % 2, t, split=t + 1 < NS, idx=t + 3 < NS)
                g = 1 + looped_units + t - LOOPED
                gather(g, more=g + 1 < GU)

        @block.tensor
        def _(pe):
            def transpose_idx(t):
                pe.wait_ge(idx_padded, t + 1)
                if not isinstance(t, int) or t > 0:
                    pe.wait_ge(idx_copied, t)
                for k in range(QK):
                    last = pe.transpose(idx_ps[:, k * P:(k + 1) * P],
                                        idx_pad[:, k, :, :].rearrange("p s j -> p (s j)").bitcast(BF16), ident_b[:, :])
                last.then_inc(idx_transposed, 1)

            def count_chunk(v, c, first=False, copied=None):
                hf = c // (CHUNKS // 2)
                if c % (CHUNKS // 2) == 0:
                    pe.wait_ge(hot_ready, 2 * v + hf + 1)
                back, lc = last_user(c)
                if not (first and back):
                    who, n, at = (act_evacuated, NA, ACT_CHUNKS) if lc in ACT_CHUNKS else (dve_evacuated, ND, DVE_CHUNKS)
                    pe.wait_ge(who, n * (v - back) + at.index(lc) + 1)
                if c == 2 and copied is not None:
                    pe.wait_ge(idx_copied, copied)
                for i in range(CP):
                    r = CP * c + i - hf * (PAIRS // 2)
                    last = pe.matmul(slots[:, c % SLOTS, i // 4, (i % 4) * P:(i % 4) * P + LOW],
                                     hot_high[0:K1, hf, r // 2, :, r % 2], hot_low[0:K1, hf, r // 2, :, r % 2],
                                     start=True, stop=True)
                last.then_inc(chunk_counted, 1)

            def sum_steps(v, k, tpar, lo, hi):
                for l in range(lo, hi):
                    last = pe.matmul(acc[k][:, 0:PARTS], counts[:, k, l, :], parts[:, tpar, l, :],
                                     start=(l == 0), stop=(l == LOW - 1))
                if hi == LOW:
                    last.then_inc(unit_summed, 1)

            CUT = [0, 0, 10, 20, 38, 52, 66, 78, LOW]

            def iteration(u, k, tpar, t, copied, more=True):
                for c in range(CHUNKS):
                    if more:
                        count_chunk(u + 1, c, copied=copied)
                    if CUT[c] == 0 and CUT[c + 1] > 0:
                        pe.wait_ge(table_split, SPLITS * (t + 1))
                        pe.wait_ge(act_evacuated, NA * (u + 1))
                        pe.wait_ge(dve_evacuated, ND * (u + 1))
                    sum_steps(u, k, tpar, CUT[c], CUT[c + 1])

            def table(tp, par, idx=True, last=False):
                t = 2 * tp + par
                if idx:
                    pe.wait_ge(act_evacuated, NA * unit(tp, par, 0, 0) + ACT_CHUNKS.index(5) + 1)
                    transpose_idx(t + 2)
                copied = t + 3 if idx else None
                loop = UNITS // 2 - (1 if last else 0)
                with pe.Fori(0, loop) as g2:
                    for k in range(2):
                        iteration(unit(tp, par, g2, k), k, par, t, copied)
                if last:
                    iteration(UT - 2, 0, par, t, copied)
                    iteration(UT - 1, 1, par, t, copied, more=False)

            pe.wait_ge(consts_ready, IDENT)
            transpose_idx(0)
            for c in range(CHUNKS):
                count_chunk(0, c, first=True, copied=1)
            pe.wait_ge(act_evacuated, ACT_CHUNKS.index(5) + 1)
            transpose_idx(1)
            pe.wait_ge(first_split, 4)
            with pe.Fori(0, LOOPED // 2) as tp:
                table(tp, 0)
                table(tp, 1)
            for t in range(LOOPED, NS):
                table(t // 2, t % 2, idx=t + 2 < NS, last=t == NS - 1)

            def tbank(i):
                return slots[:, (i % 4) // 2, i % 2, :]

            def transposed(i, prior_act, prior_dve, blocks, rows):
                need = (i - 4) // 2 + 1 if i >= 4 else 0
                done, prior = (act_copied, prior_act) if i % 2 == 0 else (dve_copied, prior_dve)
                if not (isinstance(prior, int) and prior + need == 0):
                    pe.wait_ge(done, prior + need)
                for j, src in enumerate(blocks):
                    n = src.shape[0]
                    last = pe.transpose(tbank(i)[0:rows, j * n:(j + 1) * n], src, ident_f[0:n, 0:n])
                last.then_inc(bank_transposed, 1)

            pe.wait_ge(ident_set, 2)
            pe.wait_ge(consts_ready, CONSTS)
            pe.wait_ge(w_loaded, 16)
            n = 0
            for b in range(NBLK):
                cols = slice(0, D) if b == 0 else slice(D + P * (b - 1), D + P * b)
                transposed(n, 0, 0, [ow1_n[:, o, cols] for o in range(4)], D if b == 0 else P)
                n += 1
            pe.wait_ge(dw_loaded, 32)
            for b in range(4):
                transposed(n, 0, 0, [dw1_n[:, o, b * P:(b + 1) * P] for o in range(4)], P)
                n += 1
            for half in range(2):
                transposed(n, 0, 0, [dw2_n[:, (2 * half + j) * P:(2 * half + j + 1) * P] for j in range(2)], P)
                n += 1
            assert n == W_BANKS and W_BANKS % 2 == 0

            pe.wait_ge(biases_loaded, 80)
            pe.wait_ge(parts_added, UT)

            def transpose_inputs(s, banks):
                for i in banks:
                    src = [x_n[:, b, i * P:(i + 1) * P] for b in range(4)] if i < DENSE_BANKS else \
                          [feat_n[:, b, (i - DENSE_BANKS) * P:(i - DENSE_BANKS + 1) * P] for b in range(4)]
                    transposed(i, W_BANKS // 2 + X_ACT * s, W_BANKS // 2 + X_DVE * s, src, P)

            def transpose_dense(s):
                pe.wait_ge(x_loaded, 16 * (s + 1))
                transpose_inputs(s, range(DENSE_BANKS))

            def super_block(s, more=True):
                def product(m, terms, rows):
                    if m == 3:
                        pe.wait_ge(layer_out, OUTS * s + 1)
                    if 4 <= m < OUTS - 1:
                        pe.wait_ge(layer_out, OUTS * s + m - 3)
                    for i, (w, x, wait) in enumerate(terms):
                        if wait is not None:
                            pe.wait_ge(layer_out, OUTS * s + wait)
                        last = pe.matmul(out_bank(m)[0:rows, :], w, x, start=(i == 0), stop=(i == len(terms) - 1))
                    last.then_inc(product_ready, 1)

                pe.wait_ge(act_copied, W_BANKS // 2 + X_ACT * s + DENSE_BANKS // 2)
                pe.wait_ge(dve_copied, W_BANKS // 2 + X_DVE * s + DENSE_BANKS // 2)
                for o in range(4):
                    product(o, [(dw1_t[:, b, o * P:(o + 1) * P], x_t[:, b, :], None) for b in range(4)], P)
                pe.wait_ge(feat_loaded, 16 * (1 + GATHERED) * (s + 1))
                transpose_inputs(s, range(DENSE_BANKS, X_BANKS))
                product(4, [(dw2_t[:, b, :], dense_hid[:, b, :], b + 1) for b in range(4)], D)
                pe.wait_ge(act_copied, W_BANKS // 2 + X_ACT * s + X_ACT)
                pe.wait_ge(dve_copied, W_BANKS // 2 + X_DVE * s + X_DVE)
                for o in range(4):
                    product(5 + o, [(ow1_t[:, b, o * P:(o + 1) * P], feat_t[:, b - 1, :], None) for b in range(1, NBLK)]
                            + [(ow1_t[0:D, 0, o * P:(o + 1) * P], dense_out, 5)], P)
                if more:
                    transpose_dense(s + 1)
                pe.wait_ge(weighted, 4 * s + 4)
                product(9, [(ones[:, :], weighted_sum, None)], 1)

            transpose_dense(0)
            with pe.Fori(0, SUPERS - 1) as s:
                super_block(s)
            super_block(SUPERS - 1, more=False)

        @block.scalar
        def _(act):
            def copy_idx(t, tpar, ever=True):
                act.wait_ge(idx_transposed, t + 1)
                if ever:
                    act.wait_ge(idx_split, t - 1)
                act.activation(idx_t[:, tpar, :], idx_ps.bitcast(U16), ACT.Copy).then_inc(idx_copied, 1)

            def evacuate(v, k):
                for c in ACT_CHUNKS:
                    act.wait_ge(chunk_counted, CHUNKS * v + c + 1)
                    act.activation(chunk_dst(k, c), chunk_src(c), ACT.Identity, bias=act_bias[:, 0:1]).then_inc(act_evacuated, 1)

            def table(tp, par, idx=True, last=False):
                t = 2 * tp + par
                if idx:
                    copy_idx(t + 2, par)
                with act.Fori(0, UNITS // 2 - (1 if last else 0)) as g2:
                    evacuate(unit(tp, par, g2, 0) + 1, 1)
                    evacuate(unit(tp, par, g2, 1) + 1, 0)
                if last:
                    evacuate(UT - 1, 1)

            copy_idx(0, 0, ever=False)
            act.wait_ge(consts_ready, BIASES)
            for hf in range(2):
                act.activation(hot_low[TAIL_ROWS, hf, :, :, :].rearrange("p b l e -> p (b l e)"),
                               bias_col[TAIL_ROWS, 0:1].to_broadcast([P - 96, BLK * LOW * 2]), ACT.Copy).then_inc(tails_set, 1)
            act.wait_ge(bias_set, 1)
            evacuate(0, 0)
            copy_idx(1, 1, ever=False)
            with act.Fori(0, LOOPED // 2) as tp:
                table(tp, 0)
                table(tp, 1)
            for t in range(LOOPED, NS):
                table(t // 2, t % 2, idx=t + 2 < NS, last=t == NS - 1)

            act.wait_ge(chunk_counted, CHUNKS * UT)
            act.dma_start(dw1_n[:, :, :], d_w1.rearrange("(b p) f -> p b f", p=P)).then_inc(dw_loaded, 16)
            act.dma_start(dw2_n[:, :], d_w2[:, :]).then_inc(dw_loaded, 16)
            act.wait_ge(unit_summed, UT - 1)
            load_dense(act, 0)
            act.wait_ge(biases_loaded, 80)
            for i in range(0, W_BANKS, 2):
                act.wait_ge(bank_transposed, i + 1)
                src, dst = weight_copy(i)
                act.activation(dst, src, ACT.Copy).then_inc(act_copied, 1)

            def copy_inputs(s, first, end):
                for i in range(first, end, 2):
                    act.wait_ge(bank_transposed, W_BANKS + X_BANKS * s + i + 1)
                    act.activation(input_dst(i), mlp_bank(i), ACT.Copy).then_inc(act_copied, 1)

            def super_block(s, more=True):
                def layer(m, dst, bias, rows):
                    act.wait_ge(product_ready, OUTS * s + m + 1)
                    act.activation(dst, out_bank(m)[0:rows, :], ACT.Relu, bias=bias).then_inc(layer_out, 1)

                for o in range(4):
                    layer(o, dense_hid[:, o, :], b1[:, o:o + 1], P)
                copy_inputs(s, DENSE_BANKS, X_BANKS)
                layer(4, dense_out, b2[:, 0:1], D)
                for o in range(4):
                    layer(5 + o, hid[:, o, :], ob1[:, o:o + 1], P)
                if more:
                    copy_inputs(s + 1, 0, DENSE_BANKS)
                layer(9, y[:, :], ob2[:, 0:1], 1)
                act.wait_ge(layer_out, OUTS * (s + 1))
                act.dma_start(out[bass.ds(s * 512, 512), :].rearrange("n a -> a n"), y[:, :]).then_inc(y_stored, 16)
                act.wait_ge(y_stored, 16 * (s + 1))

            copy_inputs(0, 0, DENSE_BANKS)
            with act.Fori(0, SUPERS - 1) as s:
                super_block(s)
            super_block(SUPERS - 1, more=False)

        @block.vector
        def _(dve):
            nset = [0]

            def split_idx(t, tpar):
                dve.wait_ge(idx_copied, t + 1)
                dve.tensor_scalar(high[:, tpar, :], idx_t[:, tpar, :], 1.0 / LOW, -(LOW - 1) / (2 * LOW),
                                  ALU.mult, ALU.add).then_inc(digit_set, 1)
                dve.wait_ge(digit_set, 2 * t + 1)
                dve.scalar_tensor_tensor(low[:, tpar, :], high[:, tpar, :], -float(LOW), idx_t[:, tpar, :],
                                         ALU.mult, ALU.add).then_inc(digit_set, 1)
                dve.wait_ge(digit_set, 2 * (t + 1))
                dve.sem_inc(idx_split, 1)

            def one_hots(n, v, hf, tpar, first, ever=True):
                if ever:
                    dve.wait_ge(chunk_counted, (CHUNKS // 2) * (n - 1))
                rows = slice(0, BIAS_ROW)

                def operands(size, part, dst):
                    a = iota[rows, 0:size, :].unsqueeze(1).to_broadcast([BIAS_ROW, BLK, size, 2])
                    b = part[rows, tpar, bass.ds(first, PAIRS // 2)].rearrange("p (b e) -> p b e", e=2) \
                        .unsqueeze(2).to_broadcast([BIAS_ROW, BLK, size, 2])
                    return dst[rows, hf, :, :, :], a, b

                dve.tensor_tensor(*operands(LOW, low, hot_low), ALU.is_equal).then_inc(low_hot, 1)
                dve.tensor_tensor(*operands(P, high, hot_high), ALU.is_equal)
                b_rows = hot_low[HALF:BIAS_ROW, hf, :, :, :].rearrange("p b l e -> p (b l e)")
                dve.wait_ge(low_hot, n + 1)
                dve.tensor_scalar(b_rows, b_rows, 65536.0, None, ALU.mult).then_inc(hot_ready, 1)

            def evacuate(v, k, c):
                if c not in DVE_CHUNKS:
                    return
                dve.wait_ge(chunk_counted, CHUNKS * v + c + 1)
                dve.tensor_scalar(chunk_dst(k, c), chunk_src(c), float(OFFSET), None, ALU.subtract).then_inc(dve_evacuated, 1)

            def add_parts(u, k, ever=True):
                dve.wait_ge(unit_summed, u + 1)
                if ever:
                    dve.wait_ge(stored[k], 8 * (u - k))
                dve.tensor_reduce(pooled[:, k, :], acc[k][:, 0:PARTS].rearrange("p (s d) -> p d s", s=3), AXX, ALU.add) \
                    .then_inc(parts_added, 1)

            def iteration(u, k, ones, add=True, ever=True):
                one_hots(2 * u + 3, u + 1, 1, *ones[0])
                if add:
                    add_parts(u - 1, 1 - k, ever)
                evacuate(u + 1, 1 - k, 3)
                if ones[1] is not None:
                    one_hots(2 * u + 4, u + 2, 0, *ones[1])

            def first_pair(g2, half, hf):
                return g2 * P + half * PAIRS + hf * (PAIRS // 2)

            def two_units(tp, par, g2, nxt, nth=None):
                iteration(unit(tp, par, g2, 0), 0, [(par, first_pair(g2, 1, 1)), (nxt[0], first_pair(nxt[1], 0, 0))],
                          add=nth != 0, ever=nth is None)
                iteration(unit(tp, par, g2, 1), 1, [(nxt[0], first_pair(nxt[1], 0, 1)), (nxt[0], first_pair(nxt[1], 1, 0))],
                          ever=nth != 0)

            def table(tp, par, split=True, first=False, last=False):
                t = 2 * tp + par
                if split:
                    split_idx(t + 1, 1 - par)
                if first:
                    two_units(0, 0, 0, (0, 1), nth=0)
                    two_units(0, 0, 1, (0, 2), nth=1)
                with dve.Fori(2 if first else 0, UNITS // 2 - 1) as g2:
                    two_units(tp, par, g2, (par, g2 + 1))
                g2 = UNITS // 2 - 1
                if not last:
                    two_units(tp, par, g2, (1 - par, 0))
                else:
                    iteration(UT - 2, 0, [(par, first_pair(g2, 1, 1)), None])
                    add_parts(UT - 2, 0)
                    add_parts(UT - 1, 1)

            dve.memset(act_bias[:, :], -float(OFFSET)).then_inc(bias_set, 1)
            dve.memset(raw[TAIL_ROWS, TAIL:LOW, :], 0.0).then_inc(raw_set, 1)
            dve.memset(hot_high[TAIL_ROWS, :, :, :, :], 1.0)
            split_idx(0, 0)
            dve.wait_ge(consts_ready, CONSTS)
            dve.wait_ge(tails_set, 1)
            one_hots(0, 0, 0, 0, first_pair(0, 0, 0), ever=False)
            dve.wait_ge(tails_set, 2)
            one_hots(1, 0, 1, 0, first_pair(0, 0, 1), ever=False)
            dve.wait_ge(table_loaded, 48)
            x = raw[:, 0:FIRST, :]
            hi, mid, lo = (parts[:, 0, 0:FIRST, i * D:(i + 1) * D] for i in range(3))
            dve.tensor_copy(hi, x).then_inc(first_split, 1)
            evacuate(0, 0, 3)
            dve.wait_ge(first_split, 1)
            dve.tensor_tensor(x, x, hi, ALU.subtract).then_inc(first_split, 1)
            dve.wait_ge(first_split, 2)
            dve.tensor_copy(mid, x).then_inc(first_split, 1)
            dve.wait_ge(first_split, 3)
            dve.tensor_tensor(lo, x, mid, ALU.subtract).then_inc(first_split, 1)
            one_hots(2, 1, 0, 0, first_pair(0, 1, 0))
            table(0, 0, first=True)
            table(0, 1)
            with dve.Fori(1, LOOPED // 2) as tp:
                table(tp, 0)
                table(tp, 1)
            for t in range(LOOPED, NS):
                table(t // 2, t % 2, split=t + 1 < NS, last=t == NS - 1)

            for i in range(1, W_BANKS, 2):
                dve.wait_ge(bank_transposed, i + 1)
                src, dst = weight_copy(i)
                dve.tensor_copy(dst, src).then_inc(dve_copied, 1)

            def copy_inputs(s, first, end):
                for i in range(first + 1, end, 2):
                    dve.wait_ge(bank_transposed, W_BANKS + X_BANKS * s + i + 1)
                    dve.tensor_copy(input_dst(i), mlp_bank(i)).then_inc(dve_copied, 1)

            def super_block(s, more=True):
                copy_inputs(s, DENSE_BANKS, X_BANKS)
                for o in range(4):
                    dve.wait_ge(layer_out, OUTS * s + 6 + o)
                    if o == 0:
                        dve.tensor_scalar(weighted_sum, hid[:, o, :], ow2[:, o:o + 1], None, ALU.mult).then_inc(weighted, 1)
                    else:
                        dve.wait_ge(weighted, 4 * s + o)
                        dve.scalar_tensor_tensor(weighted_sum, hid[:, o, :], ow2[:, o:o + 1], weighted_sum,
                                                 ALU.mult, ALU.add).then_inc(weighted, 1)
                if more:
                    copy_inputs(s + 1, 0, DENSE_BANKS)

            copy_inputs(0, 0, DENSE_BANKS)
            with dve.Fori(0, SUPERS - 1) as s:
                super_block(s)
            super_block(SUPERS - 1, more=False)


_INS = ['r_dense_features', 'r_sparse_features', 'L0_rec_emb_tables', 'L0_rec_d_w1', 'L0_rec_d_b1', 'L0_rec_d_w2',
        'L0_rec_d_b2', 'L0_rec_o_w1', 'L0_rec_o_b1', 'L0_rec_o_w2', 'L0_rec_o_b2']


def kernel(**inputs):
    import numpy as _np
    import concourse.bacc as _bacc
    from concourse import mybir as _mybir
    from concourse.bass_utils import run_bass_kernel_spmd as _run

    nc = _bacc.Bacc("TRN2", target_bir_lowering=False, num_devices=1)
    arrays, args = {}, []
    for name in _INS:
        a = _np.ascontiguousarray(inputs[name])
        arrays[f"in_{name}_dram"] = a
        args.append(nc.dram_tensor(f"in_{name}_dram", a.shape, _mybir.dt.from_np(a.dtype), kind="ExternalInput").ap())
    rows = inputs['r_dense_features'].shape[0]
    out = nc.dram_tensor("out_0_dram", (rows, 1), _mybir.dt.float32, kind="ExternalOutput").ap()
    build(nc, *args, out)
    r = _run(nc, [arrays], core_ids=[0])
    return r.results[0]["out_0_dram"]
```
